# Optimizing a Trainium2 kernel written in Bass

```python
import numpy as np
import jax
import jax.numpy as jnp

def _softmax(x, axis=-1):
    return jax.nn.softmax(x, axis=axis)

def _gelu(x):
    return jax.nn.gelu(x, approximate=True)

def _silu(x):
    return jax.nn.silu(x)

def _sigmoid(x):
    return jax.nn.sigmoid(x)

def _layernorm(x, axis=-1, eps=1e-05):
    m = jnp.mean(x, axis=axis, keepdims=True)
    v = jnp.var(x, axis=axis, keepdims=True)
    return (x - m) / jnp.sqrt(v + eps)

def _scatter_add(tgt, idx, src, axis=0):
    return tgt.at[idx].add(src)

def _segment_sum(src, seg, n):
    return jax.ops.segment_sum(src, seg, n)
kernel_name = 'mk_dlrm_tower_d1_rec_r8_acc687'

def setup_inputs(seed: int=0):
    np.random.seed(seed)
    _w = jnp.asarray

    def _rec_inputs():
        import jax
        import jax.numpy as jnp
        _tk = jax.random.key(seed)
        ids = jnp.stack([jax.random.randint(jax.random.fold_in(_tk, 200 + f), (512,), 0, v, jnp.int32) for f, v in enumerate([1000, 1250, 1000, 12500, 1000, 1250, 125000, 1250, 1250, 1000, 1250, 1250, 1250, 12500, 1000, 1000, 1000, 1250, 1000, 12500, 1250, 1250, 12500, 1250, 1250, 1000])], axis=1)
        tbl_0 = 0.05 * jax.random.normal(jax.random.fold_in(_tk, 500 + 0), (1000, 128), jnp.float32)
        tbl_1 = 0.05 * jax.random.normal(jax.random.fold_in(_tk, 500 + 1), (1250, 128), jnp.float32)
        tbl_2 = 0.05 * jax.random.normal(jax.random.fold_in(_tk, 500 + 2), (1000, 128), jnp.float32)
        tbl_3 = 0.05 * jax.random.normal(jax.random.fold_in(_tk, 500 + 3), (12500, 128), jnp.float32)
        tbl_4 = 0.05 * jax.random.normal(jax.random.fold_in(_tk, 500 + 4), (1000, 128), jnp.float32)
        tbl_5 = 0.05 * jax.random.normal(jax.random.fold_in(_tk, 500 + 5), (1250, 128), jnp.float32)
        tbl_6 = 0.05 * jax.random.normal(jax.random.fold_in(_tk, 500 + 6), (125000, 128), jnp.float32)
        tbl_7 = 0.05 * jax.random.normal(jax.random.fold_in(_tk, 500 + 7), (1250, 128), jnp.float32)
        tbl_8 = 0.05 * jax.random.normal(jax.random.fold_in(_tk, 500 + 8), (1250, 128), jnp.float32)
        tbl_9 = 0.05 * jax.random.normal(jax.random.fold_in(_tk, 500 + 9), (1000, 128), jnp.float32)
        tbl_10 = 0.05 * jax.random.normal(jax.random.fold_in(_tk, 500 + 10), (1250, 128), jnp.float32)
        tbl_11 = 0.05 * jax.random.normal(jax.random.fold_in(_tk, 500 + 11), (1250, 128), jnp.float32)
        tbl_12 = 0.05 * jax.random.normal(jax.random.fold_in(_tk, 500 + 12), (1250, 128), jnp.float32)
        tbl_13 = 0.05 * jax.random.normal(jax.random.fold_in(_tk, 500 + 13), (12500, 128), jnp.float32)
        tbl_14 = 0.05 * jax.random.normal(jax.random.fold_in(_tk, 500 + 14), (1000, 128), jnp.float32)
        tbl_15 = 0.05 * jax.random.normal(jax.random.fold_in(_tk, 500 + 15), (1000, 128), jnp.float32)
        tbl_16 = 0.05 * jax.random.normal(jax.random.fold_in(_tk, 500 + 16), (1000, 128), jnp.float32)
        tbl_17 = 0.05 * jax.random.normal(jax.random.fold_in(_tk, 500 + 17), (1250, 128), jnp.float32)
        tbl_18 = 0.05 * jax.random.normal(jax.random.fold_in(_tk, 500 + 18), (1000, 128), jnp.float32)
        tbl_19 = 0.05 * jax.random.normal(jax.random.fold_in(_tk, 500 + 19), (12500, 128), jnp.float32)
        tbl_20 = 0.05 * jax.random.normal(jax.random.fold_in(_tk, 500 + 20), (1250, 128), jnp.float32)
        tbl_21 = 0.05 * jax.random.normal(jax.random.fold_in(_tk, 500 + 21), (1250, 128), jnp.float32)
        tbl_22 = 0.05 * jax.random.normal(jax.random.fold_in(_tk, 500 + 22), (12500, 128), jnp.float32)
        tbl_23 = 0.05 * jax.random.normal(jax.random.fold_in(_tk, 500 + 23), (1250, 128), jnp.float32)
        tbl_24 = 0.05 * jax.random.normal(jax.random.fold_in(_tk, 500 + 24), (1250, 128), jnp.float32)
        tbl_25 = 0.05 * jax.random.normal(jax.random.fold_in(_tk, 500 + 25), (1000, 128), jnp.float32)
        _rk = jax.random.fold_in(_tk, 7)
        r_dense_x = -0.000514642 + 1.00011 * jax.random.normal(jax.random.fold_in(_rk, 101), (512, 128), jnp.float32)
        W_top1 = 0.0456912 * jax.random.normal(jax.random.fold_in(_tk, 801), (479, 512), jnp.float32)
        W_top2 = 0.0441942 * jax.random.normal(jax.random.fold_in(_tk, 802), (512, 256), jnp.float32)
        W_top3 = 0.0625 * jax.random.normal(jax.random.fold_in(_tk, 803), (256, 1), jnp.float32)
        b_top1 = jnp.zeros((512,), jnp.float32)
        b_top2 = jnp.zeros((256,), jnp.float32)
        return (r_dense_x, ids, tbl_0, tbl_1, tbl_2, tbl_3, tbl_4, tbl_5, tbl_6, tbl_7, tbl_8, tbl_9, tbl_10, tbl_11, tbl_12, tbl_13, tbl_14, tbl_15, tbl_16, tbl_17, tbl_18, tbl_19, tbl_20, tbl_21, tbl_22, tbl_23, tbl_24, tbl_25, W_top1, b_top1, W_top2, b_top2, W_top3)
    r_dense_x, ids, tbl_0, tbl_1, tbl_2, tbl_3, tbl_4, tbl_5, tbl_6, tbl_7, tbl_8, tbl_9, tbl_10, tbl_11, tbl_12, tbl_13, tbl_14, tbl_15, tbl_16, tbl_17, tbl_18, tbl_19, tbl_20, tbl_21, tbl_22, tbl_23, tbl_24, tbl_25, W_top1, b_top1, W_top2, b_top2, W_top3 = _rec_inputs()

    def _L0_rec_setup():
        import jax, jax.numpy as jnp
        import numpy as np
        F = 26
        D = 128
        B = 2048
        _TRIU_I, _TRIU_J = np.triu_indices(F + 1, k=1)
        _TRIU_I = jnp.asarray(_TRIU_I)
        _TRIU_J = jnp.asarray(_TRIU_J)
        key = jax.random.key(seed)
        k1, k2 = jax.random.split(key)
        sparse_x = jax.random.normal(k1, (B, F, D), dtype=jnp.float32)
        dense_x = jax.random.normal(k2, (B, D), dtype=jnp.float32)
        return {'sparse_x': sparse_x, 'dense_x': dense_x}
    _L0_rec_all = _L0_rec_setup()
    _L0_rec_in = {k: v for k, v in _L0_rec_all.items() if k in ()}
    del _L0_rec_all
    return {'r_dense_x': r_dense_x, 'ids': ids, 'tbl_0': tbl_0, 'tbl_1': tbl_1, 'tbl_2': tbl_2, 'tbl_3': tbl_3, 'tbl_4': tbl_4, 'tbl_5': tbl_5, 'tbl_6': tbl_6, 'tbl_7': tbl_7, 'tbl_8': tbl_8, 'tbl_9': tbl_9, 'tbl_10': tbl_10, 'tbl_11': tbl_11, 'tbl_12': tbl_12, 'tbl_13': tbl_13, 'tbl_14': tbl_14, 'tbl_15': tbl_15, 'tbl_16': tbl_16, 'tbl_17': tbl_17, 'tbl_18': tbl_18, 'tbl_19': tbl_19, 'tbl_20': tbl_20, 'tbl_21': tbl_21, 'tbl_22': tbl_22, 'tbl_23': tbl_23, 'tbl_24': tbl_24, 'tbl_25': tbl_25, 'W_top1': W_top1, 'b_top1': b_top1, 'W_top2': W_top2, 'b_top2': b_top2, 'W_top3': W_top3}

def reference(r_dense_x, ids, tbl_0, tbl_1, tbl_2, tbl_3, tbl_4, tbl_5, tbl_6, tbl_7, tbl_8, tbl_9, tbl_10, tbl_11, tbl_12, tbl_13, tbl_14, tbl_15, tbl_16, tbl_17, tbl_18, tbl_19, tbl_20, tbl_21, tbl_22, tbl_23, tbl_24, tbl_25, W_top1, b_top1, W_top2, b_top2, W_top3):
    import jax
    import jax.numpy as jnp

    def _L0_rec_ref(sparse_x, dense_x):
        import jax, jax.numpy as jnp
        import numpy as np
        F = 26
        D = 128
        B = 2048
        _TRIU_I, _TRIU_J = np.triu_indices(F + 1, k=1)
        _TRIU_I = jnp.asarray(_TRIU_I)
        _TRIU_J = jnp.asarray(_TRIU_J)
        combined = jnp.concatenate([sparse_x, dense_x[:, None, :]], axis=1)
        interact = jnp.einsum('bfd,bgd->bfg', combined, combined)
        return interact[:, _TRIU_I, _TRIU_J]
    e = jnp.stack([tbl_0[ids[:, 0]], tbl_1[ids[:, 1]], tbl_2[ids[:, 2]], tbl_3[ids[:, 3]], tbl_4[ids[:, 4]], tbl_5[ids[:, 5]], tbl_6[ids[:, 6]], tbl_7[ids[:, 7]], tbl_8[ids[:, 8]], tbl_9[ids[:, 9]], tbl_10[ids[:, 10]], tbl_11[ids[:, 11]], tbl_12[ids[:, 12]], tbl_13[ids[:, 13]], tbl_14[ids[:, 14]], tbl_15[ids[:, 15]], tbl_16[ids[:, 16]], tbl_17[ids[:, 17]], tbl_18[ids[:, 18]], tbl_19[ids[:, 19]], tbl_20[ids[:, 20]], tbl_21[ids[:, 21]], tbl_22[ids[:, 22]], tbl_23[ids[:, 23]], tbl_24[ids[:, 24]], tbl_25[ids[:, 25]]], axis=1)
    z = _L0_rec_ref(e, r_dense_x)
    z = z.reshape(z.shape[0], -1)
    h = jnp.concatenate([z, r_dense_x], axis=1)
    h = jnp.maximum(h @ W_top1 + b_top1, 0.0)
    h = jnp.maximum(h @ W_top2 + b_top2, 0.0)
    y = h @ W_top3
    return y

_drawn_inputs = setup_inputs


def setup_inputs(seed=0):
    import zlib

    import numpy as np

    out = dict(_drawn_inputs(seed))
    spreads = {'b_top1': (0.0, 0.1), 'b_top2': (0.0, 0.1)}
    factors = {}
    for name, (base, spread) in spreads.items():
        noise = np.random.default_rng([zlib.crc32(name.encode()), seed]).standard_normal(out[name].shape)
        drawn = base * np.exp(spread * noise) if base else spread * noise
        out[name] = jnp.asarray(drawn.astype(out[name].dtype))
    for name, factor in factors.items():
        out[name] = (out[name] * factor).astype(out[name].dtype)
    return out
```

```python
from contextlib import ExitStack

import concourse.bass as bass
from concourse import mybir
from concourse.alu_op_type import AluOpType as ALU

F32 = mybir.dt.float32
F32R = mybir.dt.float32r
I32 = mybir.dt.int32
ACT = mybir.ActivationFunctionType

P = 128
BATCH, DIM = 512, 128
FEATS = 26
SLOTS = FEATS + 1
HID1, HID2 = 512, 256
PAIRS = SLOTS * (SLOTS - 1) // 2

ROWS = [1000, 1250, 1000, 12500, 1000, 1250, 125000, 1250, 1250, 1000, 1250, 1250, 1250,
        12500, 1000, 1000, 1000, 1250, 1000, 12500, 1250, 1250, 12500, 1250, 1250, 1000]

NUM_SELECTED = 10
SELECTED = sorted(range(FEATS), key=lambda f: (ROWS[f], f))[:NUM_SELECTED]
GATHERED = [f for f in range(FEATS) if f not in SELECTED]
FEATURE_OF = SELECTED + GATHERED + [FEATS]

TABLE_PARTS = 125
SPRAY = 112
MAX_CHUNKS = max(ROWS[f] for f in SELECTED) // TABLE_PARTS

TILES = BATCH // P
QUAD = 32
PER_GROUP = P // QUAD
GROUPS = P // PER_GROUP
COLS = SLOTS - 1
BANK = 512
GROUPS_PER_BANK = 4
GROUPS_PER_SET = 8
SETS = GROUPS // GROUPS_PER_SET

PACK = 4
PACKS = -(-len(GATHERED) // PACK)

LOW = SLOTS // 2
RECT = LOW * (SLOTS - LOW)
PAIR_CHUNKS = [(k, min(P, PAIRS - k)) for k in range(0, PAIRS, P)]
K1 = len(PAIR_CHUNKS) + 1
M1, M2 = HID1 // P, HID2 // P


def pair_order():
    order = [(i, j) for j in range(LOW, SLOTS) for i in range(LOW)]
    for m in range(1, SLOTS - LOW):
        if m < LOW:
            order += [(i, m) for i in range(m)]
        order += [(LOW + i, LOW + m) for i in range(m)]
    return order


def first_layer_rows():
    rows = []
    for s, u in pair_order():
        i, j = sorted((FEATURE_OF[s], FEATURE_OF[u]))
        rows.append(i * SLOTS - i * (i + 1) // 2 + j - i - 1)
    return rows + list(range(PAIRS, PAIRS + DIM))


EARLY = [[], [], [0], [1], [], [2], [3], [], [4], [5, 6, 7]]
NUM_EARLY = sum(map(len, EARLY))


def dlrm_kernel(nc, x_t, ids, ids_t, tables, w1, w2, small, y):
    chunks = [ROWS[f] // TABLE_PARTS for f in SELECTED]
    onehots_before = [sum(chunks[:k]) for k in range(NUM_SELECTED + 1)]
    RAW, SPLIT, HOT = 3, 2, 12
    IDS = 3

    with ExitStack() as ctx:
        def sb(name, shape, dt=F32):
            return ctx.enter_context(nc.sbuf_tensor(name, shape, dt))

        def ps(name, shape):
            return ctx.enter_context(nc.psum_tensor(name, shape, F32))

        def sem(name):
            return ctx.enter_context(nc.semaphore(name))

        ident = sb("ident", [P, P])
        row_of = sb("row_of", [P, 2, MAX_CHUNKS])
        ids_sb = sb("ids_sb", [P, TILES, FEATS], I32)
        ids_row = sb("ids_row", [P, IDS, BATCH], I32)
        raw = sb("raw", [P, RAW, MAX_CHUNKS, DIM])
        high = sb("high", [P, SPLIT, MAX_CHUNKS, DIM], F32R)
        low = sb("low", [P, SPLIT, MAX_CHUNKS, DIM], F32R)
        hot = sb("hot", [P, HOT, BATCH], F32R)
        gathered = sb("gathered", [P, TILES, len(GATHERED), DIM])
        vecs = sb("vecs", [DIM, TILES, GROUPS, PER_GROUP, QUAD])
        xt_sb = sb("xt_sb", [DIM, BATCH])
        inter = sb("inter", [P, 2, COLS, GROUPS])
        square_room = sb("square_room", [P, (COLS + LOW + 1) * QUAD])
        square = square_room[:, 0:COLS * QUAD].rearrange("p (j i) -> p j i", i=QUAD)
        packed = sb("packed", [P, 2, PAIRS])
        pairs_t = sb("pairs_t", [P, 2, len(PAIR_CHUNKS), P])
        h1 = sb("h1", [P, M1, P])
        h2 = sb("h2", [P, M2, P])
        w1_sb = sb("w1_sb", [P, K1, HID1])
        w2_sb = sb("w2_sb", [P, M1, HID2])
        small_sb = sb("small_sb", [P, M1 + 2 * M2])
        b1_sb, b2_sb, w3_sb = small_sb[:, 0:M1], small_sb[:, M1:M1 + M2], small_sb[:, M1 + M2:]
        y_sb = sb("y_sb", [1, BATCH])

        ps_embed = ps("ps_embed", [P, 2, BANK])
        ps_trans = ps("ps_trans", [P, 2, BANK])
        ps_inter = ps("ps_inter", [P, 2, 2, BANK])
        ps_h1 = ps_embed[:, 0, :].rearrange("p (m b) -> p m b", m=M1)
        ps_h2 = ps_embed[:, 1, 0:M2 * P].rearrange("p (m b) -> p m b", m=M2)
        ps_y = ps_embed[0:1, 1, M2 * P:M2 * P + P]

        ids_loaded = sem("ids_loaded")
        x_loaded = sem("x_loaded")
        weights_loaded = sem("weights_loaded")
        table_loaded = [sem(f"table_loaded{i}") for i in range(RAW)]
        ids_row_loaded = [sem(f"ids_row_loaded{i}") for i in range(IDS)]
        pack_gathered = [sem(f"pack_gathered{i}") for i in range(TILES * PACKS)]
        consts_ready = sem("consts_ready")
        pads_zeroed = sem("pads_zeroed")
        high_ready = sem("high_ready")
        low_ready = sem("low_ready")
        hot_ready = sem("hot_ready")
        hot_used = sem("hot_used")
        embed_ready = sem("embed_ready")
        embed_stored = sem("embed_stored")
        dense_stored = sem("dense_stored")
        trans_ready = sem("trans_ready")
        trans_stored = sem("trans_stored")
        inter_ready = sem("inter_ready")
        inter_stored_dve = sem("inter_stored_dve")
        inter_stored_act = sem("inter_stored_act")
        squared = sem("squared")
        pairs_packed = sem("pairs_packed")
        h1_ready = sem("h1_ready")
        h1_stored = sem("h1_stored")
        h2_ready = sem("h2_ready")
        h2_stored = sem("h2_stored")
        y_ready = sem("y_ready")
        y_copied = sem("y_copied")
        y_written = sem("y_written")
        block = ctx.enter_context(nc.Block())

        def pack_features(n):
            t, g = divmod(n, PACKS)
            return t, g * PACK, min((g + 1) * PACK, len(GATHERED))

        def late_packs(t):
            if t + 1 >= TILES:
                return []
            return [n for n in range((t + 1) * PACKS, (t + 2) * PACKS) if n >= NUM_EARLY]

        def first_packs():
            return [n for n in range(PACKS) if n >= NUM_EARLY]

        def slot_of_all(s):
            return vecs[:, :, :, :, s].rearrange("d t g r -> d t r g")

        def by_group(columns):
            return columns.rearrange("p (t r g) -> p t r g", t=TILES, g=GROUPS)

        def inter_block(t, s, r):
            n = t * SETS + s
            q = slice(r * QUAD, (r + 1) * QUAD)
            out = inter[q, t % 2, :, s * GROUPS_PER_SET:(s + 1) * GROUPS_PER_SET].rearrange(
                "p j (a g) -> p a g j", a=2)
            src = ps_inter[q, n % 2, :, 0:GROUPS_PER_BANK * PER_GROUP * COLS].rearrange(
                "p a (g r j) -> p a g r j", g=GROUPS_PER_BANK, r=PER_GROUP)[:, :, :, r]
            return out, src

        @block.sync
        def _(sp):
            def load_table(k):
                f, c = SELECTED[k], chunks[k]
                if k >= RAW:
                    sp.wait_ge(low_ready, k - RAW + 1)
                src = tables[f].rearrange("(p c) d -> p c d", c=c)
                sp.dma_start(raw[0:SPRAY, k % RAW, 0:c], src[0:SPRAY]).then_inc(table_loaded[k % RAW], 16)
                sp.dma_start(raw[SPRAY:TABLE_PARTS, k % RAW, 0:c],
                             src[SPRAY:TABLE_PARTS]).then_inc(table_loaded[k % RAW], 16)

            def load_ids_row(k):
                if k >= IDS:
                    sp.wait_ge(hot_ready, onehots_before[k - IDS + 1])
                f = SELECTED[k]
                sp.dma_start(ids_row[:, k % IDS], ids_t[f:f + 1, :].broadcast_to([P, BATCH])
                             ).then_inc(ids_row_loaded[k % IDS], 16)

            sp.dma_start(ids_sb[:], ids.rearrange("(t p) f -> p t f", p=P)).then_inc(ids_loaded, 16)
            for k in range(2):
                load_ids_row(k)
                load_table(k)
            sp.dma_start(xt_sb[:], x_t).then_inc(x_loaded, 16)
            for k in range(2, 4):
                load_ids_row(k)
                load_table(k)
            for c, (k0, n) in enumerate(PAIR_CHUNKS):
                sp.dma_start(w1_sb[0:n, c], w1[k0:k0 + n]).then_inc(weights_loaded, 16)
            sp.dma_start(w1_sb[:, K1 - 1], w1[PAIRS:PAIRS + DIM]).then_inc(weights_loaded, 16)
            sp.dma_start(w2_sb[:], w2.rearrange("(c p) n -> p c n", p=P)).then_inc(weights_loaded, 16)
            sp.dma_start(small_sb[:], small).then_inc(weights_loaded, 16)
            for k in range(4, NUM_SELECTED):
                load_ids_row(k)
                load_table(k)
            sp.wait_ge(y_copied, TILES)
            sp.dma_start(y, y_sb[:]).then_inc(y_written, 16)
            sp.wait_ge(y_written, 16)

        WEIGHT_DMAS = len(PAIR_CHUNKS) + 3

        @block.gpsimd
        def _(pool):
            def gather(n):
                t, f0, f1 = pack_features(n)
                for f in range(f0, f1):
                    table = tables[GATHERED[f]]
                    nc.gpsimd.indirect_dma_start(
                        gathered[:, t, f], None, table,
                        bass.IndirectOffsetOnAxis(ids_sb[:, t, GATHERED[f]:GATHERED[f] + 1], 0),
                    ).then_inc(pack_gathered[n], 16)

            for kind, c in enumerate(sorted(set(chunks))):
                nc.gpsimd.iota(row_of[:, kind, 0:c], [[1, c]], base=0, channel_multiplier=c,
                               allow_small_or_imprecise_dtypes=True).then_inc(consts_ready, 1)
            nc.gpsimd.memset(ident[:], 1.0).then_inc(consts_ready, 1)
            pool.wait_ge(consts_ready, len(set(chunks)) + 1)
            nc.gpsimd.affine_select(ident[:], ident[:], pattern=[[-1, P]], compare_op=ALU.is_equal,
                                    fill=0.0, base=0, channel_multiplier=1).then_inc(consts_ready, 1)
            pool.wait_ge(ids_loaded, 16)
            for n in range(TILES * PACKS):
                gather(n)

        NUM_CONSTS = len(set(chunks)) + 2

        @block.tensor
        def _(pe):
            trans_uses = [0]

            def trans_bank():
                n = trans_uses[0]
                trans_uses[0] += 1
                if n >= 2:
                    pe.wait_ge(trans_stored, n - 1)
                return ps_trans[:, n % 2, :].rearrange("p (f b) -> p f b", b=P)

            def transpose_pack(n):
                t, f0, f1 = pack_features(n)
                pe.wait_ge(pack_gathered[n], 16 * (f1 - f0))
                bank = trans_bank()
                for f in range(f0, f1):
                    last = nc.tensor.transpose(bank[:, f - f0], gathered[:, t, f], ident[:])
                last.then_inc(trans_ready, 1)

            def select(k):
                if k >= 2:
                    pe.wait_ge(embed_stored, k - 1)
                pe.wait_ge(high_ready, k + 1)
                pe.wait_ge(low_ready, k + 1)
                for c in range(chunks[k]):
                    n = onehots_before[k] + c
                    pe.wait_ge(hot_ready, n + 1)
                    column = hot[0:TABLE_PARTS, n % HOT]
                    nc.tensor.matmul(ps_embed[:, k % 2], high[0:TABLE_PARTS, k % SPLIT, c], column,
                                     start=(c == 0), stop=False)
                    last = nc.tensor.matmul(ps_embed[:, k % 2], low[0:TABLE_PARTS, k % SPLIT, c], column,
                                            start=False, stop=(c == chunks[k] - 1))
                    last.then_inc(hot_used, 1)

            def interact(t, s):
                n = t * SETS + s
                if n >= 2:
                    pe.wait_ge(inter_stored_dve, n - 1)
                    pe.wait_ge(inter_stored_act, n - 1)
                for g in range(GROUPS_PER_SET):
                    group = vecs[:, t, s * GROUPS_PER_SET + g]
                    bank, at = divmod(g, GROUPS_PER_BANK)
                    width = PER_GROUP * COLS
                    last = nc.tensor.matmul(
                        ps_inter[:, n % 2, bank, at * width:(at + 1) * width],
                        group, group[:, :, 1:SLOTS],
                        start=True, stop=True)
                last.then_inc(inter_ready, 1)

            def transpose_pairs(t):
                pe.wait_ge(pairs_packed, t + 1)
                bank = trans_bank()
                for c, (k0, n) in enumerate(PAIR_CHUNKS):
                    last = nc.tensor.transpose(bank[0:n, c], packed[:, t % 2, k0:k0 + n], ident[:])
                last.then_inc(trans_ready, 1)
                return trans_uses[0]

            def layer1(t, pairs_use):
                if t == 0:
                    pe.wait_ge(weights_loaded, 16 * WEIGHT_DMAS)
                    pe.wait_ge(embed_stored, NUM_SELECTED)
                else:
                    pe.wait_ge(h1_stored, t)
                pe.wait_ge(trans_stored, pairs_use)
                for m in range(M1):
                    cols = slice(m * P, (m + 1) * P)
                    for c, (k0, n) in enumerate(PAIR_CHUNKS):
                        nc.tensor.matmul(ps_h1[:, m], w1_sb[0:n, c, cols], pairs_t[0:n, t % 2, c],
                                         start=(c == 0), stop=False)
                    last = nc.tensor.matmul(ps_h1[:, m], w1_sb[:, K1 - 1, cols],
                                            xt_sb[:, t * P:(t + 1) * P], start=False, stop=True)
                last.then_inc(h1_ready, 1)

            def layer2(t):
                if t >= 1:
                    pe.wait_ge(h2_stored, t)
                    pe.wait_ge(y_copied, t)
                pe.wait_ge(h1_stored, t + 1)
                for m in range(M2):
                    for c in range(M1):
                        last = nc.tensor.matmul(ps_h2[:, m], w2_sb[:, c, m * P:(m + 1) * P], h1[:, c],
                                                start=(c == 0), stop=(c == M1 - 1))
                last.then_inc(h2_ready, 1)

            def layer3(t):
                pe.wait_ge(h2_stored, t + 1)
                for c in range(M2):
                    last = nc.tensor.matmul(ps_y, w3_sb[:, c:c + 1], h2[:, c],
                                            start=(c == 0), stop=(c == M2 - 1))
                last.then_inc(y_ready, 1)

            pe.wait_ge(consts_ready, NUM_CONSTS)
            for k in range(NUM_SELECTED):
                select(k)
                for n in EARLY[k]:
                    transpose_pack(n)
            for n in first_packs():
                transpose_pack(n)
            pe.wait_ge(pads_zeroed, 1)
            pe.wait_ge(dense_stored, 1)
            pe.wait_ge(embed_stored, NUM_SELECTED)
            pairs_use = {}
            uses_before_tile = {0: trans_uses[0]}
            for t in range(TILES):
                pe.wait_ge(trans_stored, uses_before_tile[t])
                late = late_packs(t)
                for s in range(SETS):
                    interact(t, s)
                    if t >= 1:
                        if s == 0 and t >= 2:
                            layer3(t - 2)
                        if s == 1:
                            pairs_use[t - 1] = transpose_pairs(t - 1)
                        if s == 2:
                            layer1(t - 1, pairs_use[t - 1])
                        if s == 3:
                            layer2(t - 1)
                    for n in late[s::SETS]:
                        transpose_pack(n)
                uses_before_tile[t + 1] = trans_uses[0]
            layer3(TILES - 2)
            last_tile = TILES - 1
            pairs_use[last_tile] = transpose_pairs(last_tile)
            layer1(last_tile, pairs_use[last_tile])
            layer2(last_tile)
            layer3(last_tile)

        @block.scalar
        def _(act):
            trans_uses = [0]

            def split_high(k):
                act.wait_ge(table_loaded[k % RAW], 32 * (k // RAW + 1))
                if k >= SPLIT:
                    act.wait_ge(hot_used, onehots_before[k - SPLIT + 1])
                nc.scalar.activation(high[0:TABLE_PARTS, k % SPLIT, 0:chunks[k]],
                                     raw[0:TABLE_PARTS, k % RAW, 0:chunks[k]],
                                     ACT.Copy).then_inc(high_ready, 1)

            def store_embed(k):
                act.wait_ge(hot_used, onehots_before[k + 1])
                nc.scalar.activation(slot_of_all(k), by_group(ps_embed[:, k % 2]), ACT.Copy).then_inc(embed_stored, 1)

            def store_pack(n):
                t, f0, f1 = pack_features(n)
                u = trans_uses[0]
                trans_uses[0] += 1
                act.wait_ge(trans_ready, u + 1)
                slot = NUM_SELECTED + f0
                out = vecs[:, t, :, :, slot:slot + f1 - f0].rearrange("d g r f -> d f r g")
                bank = ps_trans[:, u % 2, 0:(f1 - f0) * P].rearrange("p (f r g) -> p f r g", f=f1 - f0, g=GROUPS)
                nc.scalar.activation(out, bank, ACT.Copy).then_inc(trans_stored, 1)

            def store_pairs(t):
                u = trans_uses[0]
                trans_uses[0] += 1
                act.wait_ge(trans_ready, u + 1)
                if t >= 2:
                    act.wait_ge(h1_ready, t - 1)
                bank = ps_trans[:, u % 2, :].rearrange("p (f b) -> p f b", b=P)
                full = len(PAIR_CHUNKS) - 1
                rest = PAIR_CHUNKS[-1][1]
                nc.scalar.activation(pairs_t[:, t % 2, 0:full], bank[:, 0:full], ACT.Copy)
                nc.scalar.activation(pairs_t[0:rest, t % 2, full], bank[0:rest, full],
                                     ACT.Copy).then_inc(trans_stored, 1)

            def store_inter(t, s):
                n = t * SETS + s
                act.wait_ge(inter_ready, n + 1)
                if s == 0 and t >= 2:
                    act.wait_ge(squared, t - 1)
                for r in (2, 3):
                    last = nc.scalar.activation(*inter_block(t, s, r), ACT.Copy)
                last.then_inc(inter_stored_act, 1)

            def store_y(t):
                act.wait_ge(y_ready, t + 1)
                nc.scalar.activation(y_sb[:, t * P:(t + 1) * P], ps_y, ACT.Copy).then_inc(y_copied, 1)

            split_high(0)
            for k in range(NUM_SELECTED):
                if k + 1 < NUM_SELECTED:
                    split_high(k + 1)
                if k == 0:
                    act.wait_ge(x_loaded, 16)
                    nc.scalar.activation(slot_of_all(SLOTS - 1), by_group(xt_sb[:]), ACT.Copy).then_inc(dense_stored, 1)
                store_embed(k)
                for n in EARLY[k]:
                    store_pack(n)
            for n in first_packs():
                store_pack(n)
            for t in range(TILES):
                late = late_packs(t)
                for s in range(SETS):
                    store_inter(t, s)
                    if t >= 1:
                        if s == 0 and t >= 2:
                            store_y(t - 2)
                        if s == 1:
                            store_pairs(t - 1)
                    for n in late[s::SETS]:
                        store_pack(n)
            store_y(TILES - 2)
            store_pairs(TILES - 1)
            store_y(TILES - 1)

        @block.vector
        def _(dve):
            def split_low(k):
                dve.wait_ge(high_ready, k + 1)
                nc.vector.tensor_sub(low[0:TABLE_PARTS, k % SPLIT, 0:chunks[k]],
                                     raw[0:TABLE_PARTS, k % RAW, 0:chunks[k]],
                                     high[0:TABLE_PARTS, k % SPLIT, 0:chunks[k]].bitcast(F32)
                                     ).then_inc(low_ready, 1)

            def make_hot(k):
                kind = sorted(set(chunks)).index(chunks[k])
                dve.wait_ge(ids_row_loaded[k % IDS], 16 * (k // IDS + 1))
                for c in range(chunks[k]):
                    n = onehots_before[k] + c
                    if n >= HOT:
                        dve.wait_ge(hot_used, n - HOT + 1)
                    nc.vector.tensor_scalar(hot[0:TABLE_PARTS, n % HOT], ids_row[0:TABLE_PARTS, k % IDS],
                                            row_of[0:TABLE_PARTS, kind, c:c + 1], None,
                                            ALU.is_equal).then_inc(hot_ready, 1)

            def store_inter(t, s):
                n = t * SETS + s
                dve.wait_ge(inter_ready, n + 1)
                for r in (0, 1):
                    last = nc.vector.tensor_copy(*inter_block(t, s, r))
                last.then_inc(inter_stored_dve, 1)

            def pack_pairs(t):
                dve.wait_ge(inter_stored_dve, SETS * (t + 1))
                dve.wait_ge(inter_stored_act, SETS * (t + 1))
                nc.vector.transpose(square, inter[:, t % 2]).then_inc(squared, 1)
                dve.wait_ge(squared, t + 1)
                out = packed[:, t % 2]
                last = nc.vector.tensor_copy(out[:, 0:RECT].rearrange("p (j i) -> p j i", i=LOW),
                                             square[:, LOW - 1:COLS, 0:LOW])
                at = RECT
                flat = square_room[:, :]
                step = LOW * QUAD + LOW
                for m in range(1, SLOTS - LOW):
                    first = (m - 1) * QUAD
                    if m < LOW:
                        out2 = out[:, at:at + 2 * m].rearrange("p (two i) -> p two i", two=2)
                        src2 = flat[:, first:first + 2 * step].rearrange("p (two x) -> p two x", two=2)
                        last = nc.vector.tensor_copy(out2, src2[:, :, 0:m])
                        at += 2 * m
                    else:
                        last = nc.vector.tensor_copy(out[:, at:at + m], flat[:, first + step:first + step + m])
                        at += m
                last.then_inc(pairs_packed, 1)

            def relu1(t):
                dve.wait_ge(h1_ready, t + 1)
                if t >= 1:
                    dve.wait_ge(h2_ready, t)
                for m in range(M1):
                    last = nc.vector.tensor_scalar(h1[:, m], ps_h1[:, m], b1_sb[:, m:m + 1], 0.0,
                                                   ALU.add, ALU.max)
                last.then_inc(h1_stored, 1)

            def relu2(t):
                dve.wait_ge(h2_ready, t + 1)
                if t >= 1:
                    dve.wait_ge(y_ready, t)
                for m in range(M2):
                    last = nc.vector.tensor_scalar(h2[:, m], ps_h2[:, m], b2_sb[:, m:m + 1], 0.0,
                                                   ALU.add, ALU.max)
                last.then_inc(h2_stored, 1)

            dve.wait_ge(consts_ready, NUM_CONSTS)
            nc.vector.memset(vecs[:].rearrange("d t g r s -> d (t g r) s")[:, :, SLOTS:QUAD], 0.0).then_inc(pads_zeroed, 1)
            for k in range(NUM_SELECTED):
                split_low(k)
                make_hot(k)
            dve.wait_ge(weights_loaded, 16 * WEIGHT_DMAS)
            for t in range(TILES):
                for s in range(SETS):
                    store_inter(t, s)
                    if t >= 1 and s == 0 and t >= 2:
                        relu2(t - 2)
                    if t >= 1 and s == 3:
                        relu1(t - 1)
                pack_pairs(t)
            relu2(TILES - 2)
            relu1(TILES - 1)
            relu2(TILES - 1)


def kernel(**inputs):
    import numpy as np
    import concourse.bacc as bacc
    from concourse.bass_utils import run_bass_kernel_spmd as run

    a = {k: np.asarray(v) for k, v in inputs.items()}
    arrays = {
        "x_t": np.ascontiguousarray(a["r_dense_x"].T),
        "ids": np.ascontiguousarray(a["ids"]),
        "ids_t": np.ascontiguousarray(a["ids"].T),
        "w1": np.ascontiguousarray(a["W_top1"][first_layer_rows()]),
        "w2": np.ascontiguousarray(a["W_top2"]),
        "small": np.ascontiguousarray(np.concatenate(
            [a["b_top1"].reshape(M1, P).T, a["b_top2"].reshape(M2, P).T, a["W_top3"].reshape(M2, P).T], axis=1)),
    }
    for f in range(FEATS):
        arrays[f"table{f}"] = np.ascontiguousarray(a[f"tbl_{f}"])

    nc = bacc.Bacc("TRN2", target_bir_lowering=False, num_devices=1)
    dram = {name: nc.dram_tensor(name, v.shape, mybir.dt.from_np(v.dtype), kind="ExternalInput").ap()
            for name, v in arrays.items()}
    y = nc.dram_tensor("y", (1, BATCH), F32, kind="ExternalOutput").ap()
    dlrm_kernel(nc, dram["x_t"], dram["ids"], dram["ids_t"], [dram[f"table{f}"] for f in range(FEATS)],
                dram["w1"], dram["w2"], dram["small"], y)
    return run(nc, [arrays], core_ids=[0]).results[0]["y"].reshape(BATCH, 1)
```

```python
from contextlib import ExitStack

import concourse.bass as bass
from concourse import mybir
from concourse.alu_op_type import AluOpType as ALU

F32 = mybir.dt.float32
F32R = mybir.dt.float32r
I32 = mybir.dt.int32
ACT = mybir.ActivationFunctionType

P = 128
BATCH, DIM = 512, 128
FEATS = 26
SLOTS = FEATS + 1
HID1, HID2 = 512, 256
PAIRS = SLOTS * (SLOTS - 1) // 2

ROWS = [1000, 1250, 1000, 12500, 1000, 1250, 125000, 1250, 1250, 1000, 1250, 1250, 1250,
        12500, 1000, 1000, 1000, 1250, 1000, 12500, 1250, 1250, 12500, 1250, 1250, 1000]

NUM_SELECTED = 9
SELECTED = sorted(range(FEATS), key=lambda f: (ROWS[f], f))[:NUM_SELECTED]
GATHERED = [f for f in range(FEATS) if f not in SELECTED]
FEATURE_OF = SELECTED + GATHERED + [FEATS]

TABLE_PARTS = 125
SPRAY = 112
MAX_CHUNKS = max(ROWS[f] for f in SELECTED) // TABLE_PARTS

TILES = BATCH // P
QUAD = 32
PER_GROUP = P // QUAD
GROUPS = P // PER_GROUP
COLS = SLOTS - 1
BANK = 512
GROUPS_PER_BANK = 4
GROUPS_PER_SET = 8
SETS = GROUPS // GROUPS_PER_SET

PACK = 4
PACKS = -(-len(GATHERED) // PACK)

LOW = SLOTS // 2
RECT = LOW * (SLOTS - LOW)
PAIR_CHUNKS = [(k, min(P, PAIRS - k)) for k in range(0, PAIRS, P)]
K1 = len(PAIR_CHUNKS) + 1
M1, M2 = HID1 // P, HID2 // P


def pair_order():
    order = [(i, j) for j in range(LOW, SLOTS) for i in range(LOW)]
    for m in range(1, SLOTS - LOW):
        if m < LOW:
            order += [(i, m) for i in range(m)]
        order += [(LOW + i, LOW + m) for i in range(m)]
    return order


def first_layer_rows():
    rows = []
    for s, u in pair_order():
        i, j = sorted((FEATURE_OF[s], FEATURE_OF[u]))
        rows.append(i * SLOTS - i * (i + 1) // 2 + j - i - 1)
    return rows + list(range(PAIRS, PAIRS + DIM))


EARLY = [[], [], [0], [1], [2], [3], [4, 5], [6], [7, 8]]
NUM_EARLY = sum(map(len, EARLY))
WARM_UP = 10


def dlrm_kernel(nc, x_t, ids, ids_t, tables, w1, w2, small, y):
    chunks = [ROWS[f] // TABLE_PARTS for f in SELECTED]
    onehots_before = [sum(chunks[:k]) for k in range(NUM_SELECTED + 1)]
    RAW, SPLIT = 3, 2
    IDS = 3

    with ExitStack() as ctx:
        def sb(name, shape, dt=F32):
            return ctx.enter_context(nc.sbuf_tensor(name, shape, dt))

        def ps(name, shape):
            return ctx.enter_context(nc.psum_tensor(name, shape, F32))

        def sem(name):
            return ctx.enter_context(nc.semaphore(name))

        ident = sb("ident", [P, P])
        row_of = sb("row_of", [P, 2, MAX_CHUNKS])
        ids_sb = sb("ids_sb", [P, TILES, FEATS], I32)
        ids_row = sb("ids_row", [P, IDS, BATCH], I32)
        raw = sb("raw", [P, RAW, MAX_CHUNKS, DIM])
        high = sb("high", [P, SPLIT, MAX_CHUNKS, DIM], F32R)
        low = sb("low", [P, SPLIT, MAX_CHUNKS, DIM], F32R)
        hot = sb("hot", [P, SPLIT, MAX_CHUNKS, BATCH], F32R)
        gathered = sb("gathered", [P, TILES, len(GATHERED), DIM])
        vecs = sb("vecs", [DIM, TILES, GROUPS, PER_GROUP, QUAD])
        xt_sb = sb("xt_sb", [DIM, BATCH])
        inter = sb("inter", [P, 2, COLS, GROUPS])
        square_room = sb("square_room", [P, (COLS + LOW + 1) * QUAD])
        square = square_room[:, 0:COLS * QUAD].rearrange("p (j i) -> p j i", i=QUAD)
        packed = sb("packed", [P, 2, PAIRS])
        pairs_t = sb("pairs_t", [P, 2, len(PAIR_CHUNKS), P])
        h1 = sb("h1", [P, M1, P])
        h2 = sb("h2", [P, M2, P])
        w1_sb = sb("w1_sb", [P, K1, HID1])
        w2_sb = sb("w2_sb", [P, M1, HID2])
        small_sb = sb("small_sb", [P, M1 + 2 * M2])
        b1_sb, b2_sb, w3_sb = small_sb[:, 0:M1], small_sb[:, M1:M1 + M2], small_sb[:, M1 + M2:]
        y_sb = sb("y_sb", [1, BATCH])

        ps_embed = ps("ps_embed", [P, 2, BANK])
        ps_trans = ps("ps_trans", [P, 2, BANK])
        ps_inter = ps("ps_inter", [P, 2, 2, BANK])
        ps_h1 = [[ps_embed[:, 0, m * P:(m + 1) * P] for m in range(M1)]] * (TILES - 1) + [
            [ps_inter[:, m // 2, m % 2, 0:P] for m in range(M1)]]
        ps_h2 = ps_embed[:, 1, 0:M2 * P].rearrange("p (m b) -> p m b", m=M2)
        ps_y = ps_embed[0:1, 1, M2 * P:M2 * P + P]

        ids_loaded = sem("ids_loaded")
        x_loaded = sem("x_loaded")
        weights_loaded = sem("weights_loaded")
        table_loaded = [sem(f"table_loaded{i}") for i in range(RAW)]
        ids_row_loaded = [sem(f"ids_row_loaded{i}") for i in range(IDS)]
        pack_gathered = [sem(f"pack_gathered{i}") for i in range(TILES * PACKS)]
        consts_ready = sem("consts_ready")
        pads_zeroed = sem("pads_zeroed")
        high_ready = sem("high_ready")
        low_ready = sem("low_ready")
        hot_ready = sem("hot_ready")
        embed_ready = sem("embed_ready")
        embed_stored = sem("embed_stored")
        dense_stored = sem("dense_stored")
        trans_ready = sem("trans_ready")
        trans_stored = sem("trans_stored")
        inter_ready = sem("inter_ready")
        inter_stored_dve = sem("inter_stored_dve")
        inter_stored_act = sem("inter_stored_act")
        squared = sem("squared")
        pairs_packed = sem("pairs_packed")
        h1_ready = sem("h1_ready")
        h1_stored = sem("h1_stored")
        h2_ready = sem("h2_ready")
        h2_stored = sem("h2_stored")
        y_ready = sem("y_ready")
        y_copied = sem("y_copied")
        y_written = sem("y_written")
        block = ctx.enter_context(nc.Block())

        def pack_features(n):
            t, g = divmod(n, PACKS)
            return t, g * PACK, min((g + 1) * PACK, len(GATHERED))

        def late_packs(t):
            if t + 1 >= TILES:
                return [[]] * SETS
            packs = [n for n in range((t + 1) * PACKS, (t + 2) * PACKS) if n >= NUM_EARLY]
            return [packs[s:s + 1] for s in range(SETS - 1)] + [packs[SETS - 1:]]

        def first_packs():
            return [n for n in range(PACKS) if n >= NUM_EARLY]

        def slot_of_all(s):
            return vecs[:, :, :, :, s].rearrange("d t g r -> d t r g")

        def by_group(columns):
            return columns.rearrange("p (t r g) -> p t r g", t=TILES, g=GROUPS)

        def inter_block(t, s, r):
            n = t * SETS + s
            q = slice(r * QUAD, (r + 1) * QUAD)
            out = inter[q, t % 2, :, s * GROUPS_PER_SET:(s + 1) * GROUPS_PER_SET].rearrange(
                "p j (a g) -> p a g j", a=2)
            src = ps_inter[q, n % 2, :, 0:GROUPS_PER_BANK * PER_GROUP * COLS].rearrange(
                "p a (g r j) -> p a g r j", g=GROUPS_PER_BANK, r=PER_GROUP)[:, :, :, r]
            return out, src

        @block.sync
        def _(sp):
            def load_table(k):
                f, c = SELECTED[k], chunks[k]
                if k >= RAW:
                    sp.wait_ge(low_ready, k - RAW + 1)
                src = tables[f].rearrange("(p c) d -> p c d", c=c)
                sp.dma_start(raw[0:SPRAY, k % RAW, 0:c], src[0:SPRAY]).then_inc(table_loaded[k % RAW], 16)
                sp.dma_start(raw[SPRAY:TABLE_PARTS, k % RAW, 0:c],
                             src[SPRAY:TABLE_PARTS]).then_inc(table_loaded[k % RAW], 16)

            def load_ids_row(k):
                if k >= IDS:
                    sp.wait_ge(hot_ready, onehots_before[k - IDS + 1])
                f = SELECTED[k]
                sp.dma_start(ids_row[:, k % IDS], ids_t[f:f + 1, :].broadcast_to([P, BATCH])
                             ).then_inc(ids_row_loaded[k % IDS], 16)

            sp.dma_start(ids_sb[:], ids.rearrange("(t p) f -> p t f", p=P)).then_inc(ids_loaded, 16)
            for k in range(2):
                load_ids_row(k)
                load_table(k)
            sp.dma_start(xt_sb[:], x_t).then_inc(x_loaded, 16)
            for k in range(2, 4):
                load_ids_row(k)
                load_table(k)
            for c, (k0, n) in enumerate(PAIR_CHUNKS):
                sp.dma_start(w1_sb[0:n, c], w1[k0:k0 + n]).then_inc(weights_loaded, 16)
            sp.dma_start(w1_sb[:, K1 - 1], w1[PAIRS:PAIRS + DIM]).then_inc(weights_loaded, 16)
            sp.dma_start(w2_sb[:], w2.rearrange("(c p) n -> p c n", p=P)).then_inc(weights_loaded, 16)
            sp.dma_start(small_sb[:], small).then_inc(weights_loaded, 16)
            for k in range(4, NUM_SELECTED):
                load_ids_row(k)
                load_table(k)
            sp.wait_ge(y_copied, TILES)
            sp.dma_start(y, y_sb[:]).then_inc(y_written, 16)
            sp.wait_ge(y_written, 16)

        WEIGHT_DMAS = len(PAIR_CHUNKS) + 3

        @block.gpsimd
        def _(pool):
            def gather(n):
                t, f0, f1 = pack_features(n)
                for f in range(f0, f1):
                    table = tables[GATHERED[f]]
                    nc.gpsimd.indirect_dma_start(
                        gathered[:, t, f], None, table,
                        bass.IndirectOffsetOnAxis(ids_sb[:, t, GATHERED[f]:GATHERED[f] + 1], 0),
                    ).then_inc(pack_gathered[n], 16)

            for kind, c in enumerate(sorted(set(chunks))):
                nc.gpsimd.iota(row_of[:, kind, 0:c], [[1, c]], base=0, channel_multiplier=c,
                               allow_small_or_imprecise_dtypes=True).then_inc(consts_ready, 1)
            nc.gpsimd.memset(ident[:], 1.0).then_inc(consts_ready, 1)
            pool.wait_ge(consts_ready, len(set(chunks)) + 1)
            nc.gpsimd.affine_select(ident[:], ident[:], pattern=[[-1, P]], compare_op=ALU.is_equal,
                                    fill=0.0, base=0, channel_multiplier=1).then_inc(consts_ready, 1)
            pool.wait_ge(ids_loaded, 16)
            for n in range(TILES * PACKS):
                gather(n)

        NUM_CONSTS = len(set(chunks)) + 2

        @block.tensor
        def _(pe):
            trans_uses = [0]

            def trans_bank():
                n = trans_uses[0]
                trans_uses[0] += 1
                if n >= 2:
                    pe.wait_ge(trans_stored, n - 1)
                return ps_trans[:, n % 2, :].rearrange("p (f b) -> p f b", b=P)

            def transpose_pack(n):
                t, f0, f1 = pack_features(n)
                pe.wait_ge(pack_gathered[n], 16 * (f1 - f0))
                bank = trans_bank()
                for f in range(f0, f1):
                    last = nc.tensor.transpose(bank[:, f - f0], gathered[:, t, f], ident[:])
                last.then_inc(trans_ready, 1)

            def select(k):
                if k >= 2:
                    pe.wait_ge(embed_stored, k - 1)
                pe.wait_ge(high_ready, k + 1)
                for c in range(chunks[k]):
                    pe.wait_ge(hot_ready, onehots_before[k] + c + 1)
                    nc.tensor.matmul(ps_embed[:, k % 2], high[0:TABLE_PARTS, k % SPLIT, c],
                                     hot[0:TABLE_PARTS, k % SPLIT, c], start=(c == 0), stop=False)
                pe.wait_ge(low_ready, k + 1)
                for c in range(chunks[k]):
                    last = nc.tensor.matmul(ps_embed[:, k % 2], low[0:TABLE_PARTS, k % SPLIT, c],
                                            hot[0:TABLE_PARTS, k % SPLIT, c],
                                            start=False, stop=(c == chunks[k] - 1))
                last.then_inc(embed_ready, 1)

            def interact(t, s):
                n = t * SETS + s
                if n >= 2:
                    pe.wait_ge(inter_stored_dve, n - 1)
                    pe.wait_ge(inter_stored_act, n - 1)
                for g in range(GROUPS_PER_SET):
                    group = vecs[:, t, s * GROUPS_PER_SET + g]
                    bank, at = divmod(g, GROUPS_PER_BANK)
                    width = PER_GROUP * COLS
                    last = nc.tensor.matmul(
                        ps_inter[:, n % 2, bank, at * width:(at + 1) * width],
                        group, group[:, :, 1:SLOTS],
                        start=True, stop=True)
                last.then_inc(inter_ready, 1)

            def transpose_pairs(t):
                pe.wait_ge(pairs_packed, t + 1)
                bank = trans_bank()
                for c, (k0, n) in enumerate(PAIR_CHUNKS):
                    last = nc.tensor.transpose(bank[0:n, c], packed[:, t % 2, k0:k0 + n], ident[:])
                last.then_inc(trans_ready, 1)
                return trans_uses[0]

            def layer1(t, pairs_use):
                if t == 0:
                    pe.wait_ge(weights_loaded, 16 * WEIGHT_DMAS)
                    pe.wait_ge(embed_stored, NUM_SELECTED)
                else:
                    pe.wait_ge(h1_stored, M1 * t)
                if t == TILES - 1:
                    pe.wait_ge(inter_stored_dve, SETS * TILES)
                    pe.wait_ge(inter_stored_act, SETS * TILES)
                pe.wait_ge(trans_stored, pairs_use)
                for m in range(M1):
                    cols = slice(m * P, (m + 1) * P)
                    for c, (k0, n) in enumerate(PAIR_CHUNKS):
                        nc.tensor.matmul(ps_h1[t][m], w1_sb[0:n, c, cols], pairs_t[0:n, t % 2, c],
                                         start=(c == 0), stop=False)
                    nc.tensor.matmul(ps_h1[t][m], w1_sb[:, K1 - 1, cols], xt_sb[:, t * P:(t + 1) * P],
                                     start=False, stop=True).then_inc(h1_ready, 1)

            def layer2(t):
                if t >= 1:
                    pe.wait_ge(h2_stored, t)
                    pe.wait_ge(y_copied, t)
                for m in range(M2):
                    for c in range(M1):
                        if m == 0:
                            pe.wait_ge(h1_stored, M1 * t + c + 1)
                        last = nc.tensor.matmul(ps_h2[:, m], w2_sb[:, c, m * P:(m + 1) * P], h1[:, c],
                                                start=(c == 0), stop=(c == M1 - 1))
                last.then_inc(h2_ready, 1)

            def layer3(t):
                pe.wait_ge(h2_stored, t + 1)
                for c in range(M2):
                    last = nc.tensor.matmul(ps_y, w3_sb[:, c:c + 1], h2[:, c],
                                            start=(c == 0), stop=(c == M2 - 1))
                last.then_inc(y_ready, 1)

            pe.wait_ge(consts_ready, NUM_CONSTS)
            for _ in range(WARM_UP):
                nc.tensor.matmul(ps_inter[:, 0, 0, 0:P], ident[:], ident[:], start=True, stop=True)
            for k in range(NUM_SELECTED):
                select(k)
                for n in EARLY[k]:
                    transpose_pack(n)
            for n in first_packs():
                transpose_pack(n)
            pe.wait_ge(pads_zeroed, 1)
            pe.wait_ge(dense_stored, 1)
            pe.wait_ge(embed_stored, NUM_SELECTED)
            pairs_use = {}
            uses_before_tile = {0: trans_uses[0]}
            for t in range(TILES):
                pe.wait_ge(trans_stored, uses_before_tile[t])
                late = late_packs(t)
                for s in range(SETS):
                    interact(t, s)
                    if s == 0 and t >= 2:
                        layer3(t - 2)
                    if s == 1 and t >= 1:
                        pairs_use[t - 1] = transpose_pairs(t - 1)
                    if s == 2 and 1 <= t < TILES - 1:
                        layer1(t - 1, pairs_use[t - 1])
                    for n in late[s]:
                        transpose_pack(n)
                    if s == 3 and 1 <= t < TILES - 1:
                        layer2(t - 1)
                uses_before_tile[t + 1] = trans_uses[0]
            t = TILES - 1
            layer1(t - 1, pairs_use[t - 1])
            pairs_use[t] = transpose_pairs(t)
            layer2(t - 1)
            layer1(t, pairs_use[t])
            layer3(t - 1)
            layer2(t)
            layer3(t)

        @block.scalar
        def _(act):
            trans_uses = [0]

            def split_high(k):
                act.wait_ge(table_loaded[k % RAW], 32 * (k // RAW + 1))
                if k >= SPLIT:
                    act.wait_ge(embed_ready, k - SPLIT + 1)
                nc.scalar.activation(high[0:TABLE_PARTS, k % SPLIT, 0:chunks[k]],
                                     raw[0:TABLE_PARTS, k % RAW, 0:chunks[k]],
                                     ACT.Copy).then_inc(high_ready, 1)

            def store_embed(k):
                act.wait_ge(embed_ready, k + 1)
                nc.scalar.activation(slot_of_all(k), by_group(ps_embed[:, k % 2]), ACT.Copy).then_inc(embed_stored, 1)

            def store_pack(n):
                t, f0, f1 = pack_features(n)
                u = trans_uses[0]
                trans_uses[0] += 1
                act.wait_ge(trans_ready, u + 1)
                slot = NUM_SELECTED + f0
                out = vecs[:, t, :, :, slot:slot + f1 - f0].rearrange("d g r f -> d f r g")
                bank = ps_trans[:, u % 2, 0:(f1 - f0) * P].rearrange("p (f r g) -> p f r g", f=f1 - f0, g=GROUPS)
                nc.scalar.activation(out, bank, ACT.Copy).then_inc(trans_stored, 1)

            def store_pairs(t):
                u = trans_uses[0]
                trans_uses[0] += 1
                act.wait_ge(trans_ready, u + 1)
                if t >= 2:
                    act.wait_ge(h1_ready, M1 * (t - 1))
                bank = ps_trans[:, u % 2, :].rearrange("p (f b) -> p f b", b=P)
                full = len(PAIR_CHUNKS) - 1
                rest = PAIR_CHUNKS[-1][1]
                nc.scalar.activation(pairs_t[:, t % 2, 0:full], bank[:, 0:full], ACT.Copy)
                nc.scalar.activation(pairs_t[0:rest, t % 2, full], bank[0:rest, full],
                                     ACT.Copy).then_inc(trans_stored, 1)

            def store_inter(t, s):
                n = t * SETS + s
                act.wait_ge(inter_ready, n + 1)
                if s == 0 and t >= 2:
                    act.wait_ge(squared, t - 1)
                for r in (2, 3):
                    last = nc.scalar.activation(*inter_block(t, s, r), ACT.Copy)
                last.then_inc(inter_stored_act, 1)

            def store_y(t):
                act.wait_ge(y_ready, t + 1)
                nc.scalar.activation(y_sb[:, t * P:(t + 1) * P], ps_y, ACT.Copy).then_inc(y_copied, 1)

            def relu1(t):
                if t >= 1:
                    act.wait_ge(h2_ready, t)
                for m in range(M1):
                    act.wait_ge(h1_ready, M1 * t + (m + 1 if t == TILES - 1 else M1))
                    nc.scalar.activation(h1[:, m], ps_h1[t][m], ACT.Relu, bias=b1_sb[:, m:m + 1]
                                         ).then_inc(h1_stored, 1)

            def relu2(t):
                act.wait_ge(h2_ready, t + 1)
                if t >= 1:
                    act.wait_ge(y_ready, t)
                for m in range(M2):
                    last = nc.scalar.activation(h2[:, m], ps_h2[:, m], ACT.Relu, bias=b2_sb[:, m:m + 1])
                last.then_inc(h2_stored, 1)

            split_high(0)
            for k in range(NUM_SELECTED):
                if k + 1 < NUM_SELECTED:
                    split_high(k + 1)
                if k == 0:
                    act.wait_ge(x_loaded, 16)
                    nc.scalar.activation(slot_of_all(SLOTS - 1), by_group(xt_sb[:]), ACT.Copy).then_inc(dense_stored, 1)
                store_embed(k)
                for n in EARLY[k]:
                    store_pack(n)
            for n in first_packs():
                store_pack(n)
            act.wait_ge(weights_loaded, 16 * WEIGHT_DMAS)
            for t in range(TILES):
                late = late_packs(t)
                for s in range(SETS):
                    if s == 3 and 1 <= t < TILES - 1:
                        relu1(t - 1)
                    if s == 0 and t >= 2:
                        relu2(t - 2)
                    store_inter(t, s)
                    if s == 0 and t >= 2:
                        store_y(t - 2)
                    if s == 1 and t >= 1:
                        store_pairs(t - 1)
                    for n in late[s]:
                        store_pack(n)
            t = TILES - 1
            relu1(t - 1)
            store_pairs(t)
            relu2(t - 1)
            relu1(t)
            store_y(t - 1)
            relu2(t)
            store_y(t)

        @block.vector
        def _(dve):
            def split_low(k):
                dve.wait_ge(high_ready, k + 1)
                nc.vector.tensor_sub(low[0:TABLE_PARTS, k % SPLIT, 0:chunks[k]],
                                     raw[0:TABLE_PARTS, k % RAW, 0:chunks[k]],
                                     high[0:TABLE_PARTS, k % SPLIT, 0:chunks[k]].bitcast(F32)
                                     ).then_inc(low_ready, 1)

            def make_hot(k):
                kind = sorted(set(chunks)).index(chunks[k])
                dve.wait_ge(ids_row_loaded[k % IDS], 16 * (k // IDS + 1))
                if k >= SPLIT:
                    dve.wait_ge(embed_ready, k - SPLIT + 1)
                for c in range(chunks[k]):
                    nc.vector.tensor_scalar(hot[0:TABLE_PARTS, k % SPLIT, c], ids_row[0:TABLE_PARTS, k % IDS],
                                            row_of[0:TABLE_PARTS, kind, c:c + 1], None,
                                            ALU.is_equal).then_inc(hot_ready, 1)

            def store_inter(t, s):
                n = t * SETS + s
                dve.wait_ge(inter_ready, n + 1)
                for r in (0, 1):
                    last = nc.vector.tensor_copy(*inter_block(t, s, r))
                last.then_inc(inter_stored_dve, 1)

            def pack_pairs(t):
                dve.wait_ge(inter_stored_dve, SETS * (t + 1))
                dve.wait_ge(inter_stored_act, SETS * (t + 1))
                nc.vector.transpose(square, inter[:, t % 2]).then_inc(squared, 1)
                dve.wait_ge(squared, t + 1)
                out = packed[:, t % 2]
                last = nc.vector.tensor_copy(out[:, 0:RECT].rearrange("p (j i) -> p j i", i=LOW),
                                             square[:, LOW - 1:COLS, 0:LOW])
                at = RECT
                flat = square_room[:, :]
                step = LOW * QUAD + LOW
                for m in range(1, SLOTS - LOW):
                    first = (m - 1) * QUAD
                    if m < LOW:
                        out2 = out[:, at:at + 2 * m].rearrange("p (two i) -> p two i", two=2)
                        src2 = flat[:, first:first + 2 * step].rearrange("p (two x) -> p two x", two=2)
                        last = nc.vector.tensor_copy(out2, src2[:, :, 0:m])
                        at += 2 * m
                    else:
                        last = nc.vector.tensor_copy(out[:, at:at + m], flat[:, first + step:first + step + m])
                        at += m
                last.then_inc(pairs_packed, 1)

            dve.wait_ge(consts_ready, NUM_CONSTS)
            nc.vector.memset(vecs[:].rearrange("d t g r s -> d (t g r) s")[:, :, SLOTS:QUAD], 0.0).then_inc(pads_zeroed, 1)
            for k in range(NUM_SELECTED):
                make_hot(k)
                split_low(k)
            for t in range(TILES):
                for s in range(SETS):
                    store_inter(t, s)
                pack_pairs(t)


def kernel(**inputs):
    import numpy as np
    import concourse.bacc as bacc
    from concourse.bass_utils import run_bass_kernel_spmd as run

    a = {k: np.asarray(v) for k, v in inputs.items()}
    arrays = {
        "x_t": np.ascontiguousarray(a["r_dense_x"].T),
        "ids": np.ascontiguousarray(a["ids"]),
        "ids_t": np.ascontiguousarray(a["ids"].T),
        "w1": np.ascontiguousarray(a["W_top1"][first_layer_rows()]),
        "w2": np.ascontiguousarray(a["W_top2"]),
        "small": np.ascontiguousarray(np.concatenate(
            [a["b_top1"].reshape(M1, P).T, a["b_top2"].reshape(M2, P).T, a["W_top3"].reshape(M2, P).T], axis=1)),
    }
    for f in range(FEATS):
        arrays[f"table{f}"] = np.ascontiguousarray(a[f"tbl_{f}"])

    nc = bacc.Bacc("TRN2", target_bir_lowering=False, num_devices=1)
    dram = {name: nc.dram_tensor(name, v.shape, mybir.dt.from_np(v.dtype), kind="ExternalInput").ap()
            for name, v in arrays.items()}
    y = nc.dram_tensor("y", (1, BATCH), F32, kind="ExternalOutput").ap()
    dlrm_kernel(nc, dram["x_t"], dram["ids"], dram["ids_t"], [dram[f"table{f}"] for f in range(FEATS)],
                dram["w1"], dram["w2"], dram["small"], y)
    return run(nc, [arrays], core_ids=[0]).results[0]["y"].reshape(BATCH, 1)
```

```python
from contextlib import ExitStack

import concourse.bass as bass
from concourse import mybir
from concourse.alu_op_type import AluOpType as ALU

F32 = mybir.dt.float32
F32R = mybir.dt.float32r
I32 = mybir.dt.int32
ACT = mybir.ActivationFunctionType

P = 128
BATCH, DIM = 512, 128
FEATS = 26
SLOTS = FEATS + 1
HID1, HID2 = 512, 256
PAIRS = SLOTS * (SLOTS - 1) // 2

ROWS = [1000, 1250, 1000, 12500, 1000, 1250, 125000, 1250, 1250, 1000, 1250, 1250, 1250,
        12500, 1000, 1000, 1000, 1250, 1000, 12500, 1250, 1250, 12500, 1250, 1250, 1000]

SELECTED = [f for f in range(FEATS) if ROWS[f] == min(ROWS)]
NUM_SELECTED = len(SELECTED)
GATHERED = [f for f in range(FEATS) if f not in SELECTED]
FEATURE_OF = SELECTED + GATHERED + [FEATS]

TABLE_PARTS = 125
CHUNKS = min(ROWS) // TABLE_PARTS
SPRAY = 112

TILES = BATCH // P
QUAD = 32
PER_GROUP = P // QUAD
GROUPS = P // PER_GROUP
COLS = SLOTS - 1
ROWS_OUT = P - QUAD + COLS
BANK = 512
GROUPS_PER_BANK = 4
GROUPS_PER_SET = 8
SETS = GROUPS // GROUPS_PER_SET

PACK = 4
PACKS = -(-len(GATHERED) // PACK)

LOW = SLOTS // 2
RECT = LOW * (SLOTS - LOW)
PAIR_CHUNKS = [(k, min(P, PAIRS - k)) for k in range(0, PAIRS, P)]
K1 = len(PAIR_CHUNKS) + 1
M1, M2 = HID1 // P, HID2 // P


def pair_order():
    order = [(i, j) for j in range(LOW, SLOTS) for i in range(LOW)]
    for m in range(1, SLOTS - LOW):
        if m < LOW:
            order += [(i, m) for i in range(m)]
        order += [(LOW + i, LOW + m) for i in range(m)]
    return order


def first_layer_rows():
    rows = []
    for s, u in pair_order():
        i, j = sorted((FEATURE_OF[s], FEATURE_OF[u]))
        rows.append(i * SLOTS - i * (i + 1) // 2 + j - i - 1)
    return rows + list(range(PAIRS, PAIRS + DIM))



EARLY = [[], [0], [1], [2], [3], [4], [5], [6], [7, 8]]
NUM_EARLY = sum(map(len, EARLY))
assert NUM_EARLY >= PACKS and len(EARLY) == NUM_SELECTED
WARM_UP = 10


def dlrm_kernel(nc, x_t, ids, ids_t, tables, w1, w2, small, y):
    DVE_HOTS = CHUNKS - 1
    RAW, SPLIT = 3, 2
    IDS = 3

    with ExitStack() as ctx:
        def sb(name, shape, dt=F32):
            return ctx.enter_context(nc.sbuf_tensor(name, shape, dt))

        def ps(name, shape):
            return ctx.enter_context(nc.psum_tensor(name, shape, F32))

        def sem(name):
            return ctx.enter_context(nc.semaphore(name))

        ident = sb("ident", [P, P])
        row_of = sb("row_of", [P, CHUNKS])
        ids_sb = sb("ids_sb", [P, TILES, FEATS], I32)
        ids_row = sb("ids_row", [P, IDS, BATCH], I32)
        raw = sb("raw", [P, RAW, CHUNKS, DIM])
        high = sb("high", [P, SPLIT, CHUNKS, DIM], F32R)
        low = sb("low", [P, SPLIT, CHUNKS, DIM], F32R)
        hot = sb("hot", [P, SPLIT, CHUNKS, BATCH], F32R)
        distance = sb("distance", [P, BATCH])
        gathered = sb("gathered", [P, TILES, len(GATHERED), DIM])
        vecs = sb("vecs", [DIM, TILES, GROUPS, PER_GROUP, QUAD])
        xt_sb = sb("xt_sb", [DIM, BATCH])
        inter = sb("inter", [P, 2, COLS, GROUPS])
        square_room = sb("square_room", [P, (COLS + LOW + 1) * QUAD])
        square = square_room[:, 0:COLS * QUAD].rearrange("p (j i) -> p j i", i=QUAD)
        packed = sb("packed", [P, 2, PAIRS])
        pairs_t = sb("pairs_t", [P, 2, len(PAIR_CHUNKS), P])
        h1 = sb("h1", [P, M1, P])
        h2 = sb("h2", [P, M2, P])
        w1_sb = sb("w1_sb", [P, K1, HID1])
        w2_sb = sb("w2_sb", [P, M1, HID2])
        small_sb = sb("small_sb", [P, M1 + 2 * M2])
        b1_sb, b2_sb, w3_sb = small_sb[:, 0:M1], small_sb[:, M1:M1 + M2], small_sb[:, M1 + M2:]
        y_sb = sb("y_sb", [1, BATCH])

        ps_embed = ps("ps_embed", [P, 2, BANK])
        ps_trans = ps("ps_trans", [P, 2, BANK])
        ps_inter = ps("ps_inter", [P, 2, 2, BANK])
        ps_h1 = [[ps_embed[:, 0, m * P:(m + 1) * P] for m in range(M1)]] * (TILES - 1) + [
            [ps_inter[:, m // 2, m % 2, 0:P] for m in range(M1)]]
        ps_h2 = [[ps_embed[:, 1, m * P:(m + 1) * P] for m in range(M2)]] * (TILES - 1) + [
            [ps_embed[:, m, 0:P] for m in range(M2)]]
        ps_y = [ps_embed[0:1, 1, M2 * P:M2 * P + P]] * (TILES - 1) + [ps_embed[0:1, 0, P:2 * P]]

        ids_loaded = sem("ids_loaded")
        x_loaded = sem("x_loaded")
        weights_loaded = sem("weights_loaded")
        table_loaded = [sem(f"table_loaded{i}") for i in range(RAW)]
        ids_row_loaded = [sem(f"ids_row_loaded{i}") for i in range(IDS)]
        pack_gathered = [sem(f"pack_gathered{i}") for i in range(TILES * PACKS)]
        consts_ready = sem("consts_ready")
        pads_zeroed = sem("pads_zeroed")
        rows_zeroed = sem("rows_zeroed")
        high_ready = sem("high_ready")
        low_ready = sem("low_ready")
        hot_ready = sem("hot_ready")
        last_hot_ready = sem("last_hot_ready")
        distance_ready = sem("distance_ready")
        embed_ready = sem("embed_ready")
        embed_stored = sem("embed_stored")
        dense_stored = sem("dense_stored")
        trans_ready = sem("trans_ready")
        trans_stored = sem("trans_stored")
        inter_ready = sem("inter_ready")
        inter_stored_dve = sem("inter_stored_dve")
        inter_stored_act = sem("inter_stored_act")
        squared = sem("squared")
        pairs_packed = sem("pairs_packed")
        h1_ready = sem("h1_ready")
        h1_stored = sem("h1_stored")
        h2_ready = sem("h2_ready")
        h2_stored = sem("h2_stored")
        y_ready = sem("y_ready")
        y_copied = sem("y_copied")
        y_written = sem("y_written")
        block = ctx.enter_context(nc.Block())

        def pack_features(n):
            t, g = divmod(n, PACKS)
            return t, g * PACK, min((g + 1) * PACK, len(GATHERED))

        def late_packs(t):
            if t + 1 >= TILES:
                return [[]] * SETS
            packs = [n for n in range((t + 1) * PACKS, (t + 2) * PACKS) if n >= NUM_EARLY]
            return [[], packs[0:1], packs[1:3], packs[3:]]

        def slot_of_all(s):
            return vecs[:, :, :, :, s].rearrange("d t g r -> d t r g")

        def by_group(columns):
            return columns.rearrange("p (t r g) -> p t r g", t=TILES, g=GROUPS)

        def inter_block(t, s, r):
            n = t * SETS + s
            q = slice(r * QUAD, min((r + 1) * QUAD, ROWS_OUT))
            out = inter[q, t % 2, :, s * GROUPS_PER_SET:(s + 1) * GROUPS_PER_SET].rearrange(
                "p j (a g) -> p a g j", a=2)
            src = ps_inter[q, n % 2, :, 0:GROUPS_PER_BANK * PER_GROUP * COLS].rearrange(
                "p a (g r j) -> p a g r j", g=GROUPS_PER_BANK, r=PER_GROUP)[:, :, :, r]
            return out, src

        @block.sync
        def _(sp):
            def load_table(k):
                if k >= RAW:
                    sp.wait_ge(low_ready, k - RAW + 1)
                src = tables[SELECTED[k]].rearrange("(p c) d -> p c d", c=CHUNKS)
                sp.dma_start(raw[0:SPRAY, k % RAW], src[0:SPRAY]).then_inc(table_loaded[k % RAW], 16)
                sp.dma_start(raw[SPRAY:TABLE_PARTS, k % RAW],
                             src[SPRAY:TABLE_PARTS]).then_inc(table_loaded[k % RAW], 16)

            def load_ids_row(k):
                if k >= IDS:
                    sp.wait_ge(hot_ready, DVE_HOTS * (k - IDS + 1))
                    sp.wait_ge(last_hot_ready, k - IDS + 1)
                f = SELECTED[k]
                sp.dma_start(ids_row[:, k % IDS], ids_t[f:f + 1, :].broadcast_to([P, BATCH])
                             ).then_inc(ids_row_loaded[k % IDS], 16)

            sp.dma_start(ids_sb[:], ids.rearrange("(t p) f -> p t f", p=P)).then_inc(ids_loaded, 16)
            for k in range(2):
                load_ids_row(k)
                load_table(k)
            sp.dma_start(xt_sb[:], x_t).then_inc(x_loaded, 16)
            for k in range(2, 4):
                load_ids_row(k)
                load_table(k)
            for c, (k0, n) in enumerate(PAIR_CHUNKS):
                sp.dma_start(w1_sb[0:n, c], w1[k0:k0 + n]).then_inc(weights_loaded, 16)
            sp.dma_start(w1_sb[:, K1 - 1], w1[PAIRS:PAIRS + DIM]).then_inc(weights_loaded, 16)
            sp.dma_start(w2_sb[:], w2.rearrange("(c p) n -> p c n", p=P)).then_inc(weights_loaded, 16)
            sp.dma_start(small_sb[:], small).then_inc(weights_loaded, 16)
            for k in range(4, NUM_SELECTED):
                load_ids_row(k)
                load_table(k)
            sp.wait_ge(y_copied, TILES)
            sp.dma_start(y, y_sb[:]).then_inc(y_written, 16)
            sp.wait_ge(y_written, 16)

        WEIGHT_DMAS = len(PAIR_CHUNKS) + 3
        NUM_CONSTS = 3

        @block.gpsimd
        def _(pool):
            def gather(n):
                t, f0, f1 = pack_features(n)
                for f in range(f0, f1):
                    table = tables[GATHERED[f]]
                    nc.gpsimd.indirect_dma_start(
                        gathered[:, t, f], None, table,
                        bass.IndirectOffsetOnAxis(ids_sb[:, t, GATHERED[f]:GATHERED[f] + 1], 0),
                    ).then_inc(pack_gathered[n], 16)

            nc.gpsimd.iota(row_of[:], [[1, CHUNKS]], base=0, channel_multiplier=CHUNKS,
                           allow_small_or_imprecise_dtypes=True).then_inc(consts_ready, 1)
            nc.gpsimd.memset(ident[:], 1.0).then_inc(consts_ready, 1)
            pool.wait_ge(consts_ready, 2)
            nc.gpsimd.affine_select(ident[:], ident[:], pattern=[[-1, P]], compare_op=ALU.is_equal,
                                    fill=0.0, base=0, channel_multiplier=1).then_inc(consts_ready, 1)
            pool.wait_ge(ids_loaded, 16)
            for n in range(TILES * PACKS):
                gather(n)

        @block.tensor
        def _(pe):
            trans_uses = [0]
            uses_at_tile = {}

            def trans_bank():
                n = trans_uses[0]
                trans_uses[0] += 1
                if n >= 2:
                    pe.wait_ge(trans_stored, n - 1)
                return ps_trans[:, n % 2, :].rearrange("p (f b) -> p f b", b=P)

            def transpose_pack(n):
                t, f0, f1 = pack_features(n)
                pe.wait_ge(pack_gathered[n], 16 * (f1 - f0))
                bank = trans_bank()
                for f in range(f0, f1):
                    last = nc.tensor.transpose(bank[:, f - f0], gathered[:, t, f], ident[:])
                last.then_inc(trans_ready, 1)
                uses_at_tile[t] = trans_uses[0]

            def select(k):
                if k >= 2:
                    pe.wait_ge(embed_stored, k - 1)
                pe.wait_ge(high_ready, k + 1)
                for c in range(CHUNKS):
                    if c < DVE_HOTS:
                        pe.wait_ge(hot_ready, DVE_HOTS * k + c + 1)
                    else:
                        pe.wait_ge(last_hot_ready, k + 1)
                    nc.tensor.matmul(ps_embed[:, k % 2], high[0:TABLE_PARTS, k % SPLIT, c],
                                     hot[0:TABLE_PARTS, k % SPLIT, c], start=(c == 0), stop=False)
                pe.wait_ge(low_ready, k + 1)
                for c in range(CHUNKS):
                    last = nc.tensor.matmul(ps_embed[:, k % 2], low[0:TABLE_PARTS, k % SPLIT, c],
                                            hot[0:TABLE_PARTS, k % SPLIT, c],
                                            start=False, stop=(c == CHUNKS - 1))
                last.then_inc(embed_ready, 1)

            def interact(t, s):
                n = t * SETS + s
                if n >= 2:
                    pe.wait_ge(inter_stored_dve, n - 1)
                    pe.wait_ge(inter_stored_act, n - 1)
                for g in range(GROUPS_PER_SET):
                    group = vecs[:, t, s * GROUPS_PER_SET + g]
                    bank, at = divmod(g, GROUPS_PER_BANK)
                    width = PER_GROUP * COLS
                    last = nc.tensor.matmul(
                        ps_inter[0:ROWS_OUT, n % 2, bank, at * width:(at + 1) * width],
                        group.rearrange("d r s -> d (r s)")[:, 0:ROWS_OUT], group[:, :, 1:SLOTS],
                        start=True, stop=True)
                last.then_inc(inter_ready, 1)

            def transpose_pairs(t):
                pe.wait_ge(pairs_packed, t + 1)
                bank = trans_bank()
                for c, (k0, n) in enumerate(PAIR_CHUNKS):
                    last = nc.tensor.transpose(bank[0:n, c], packed[:, t % 2, k0:k0 + n], ident[:])
                last.then_inc(trans_ready, 1)
                return trans_uses[0]

            def layer1(t, pairs_use):
                if t == 0:
                    pe.wait_ge(weights_loaded, 16 * WEIGHT_DMAS)
                    pe.wait_ge(embed_stored, NUM_SELECTED)
                else:
                    pe.wait_ge(h1_stored, M1 * t)
                if t == TILES - 1:
                    pe.wait_ge(inter_stored_dve, SETS * TILES)
                    pe.wait_ge(inter_stored_act, SETS * TILES)
                pe.wait_ge(trans_stored, pairs_use)
                for m in range(M1):
                    cols = slice(m * P, (m + 1) * P)
                    for c, (k0, n) in enumerate(PAIR_CHUNKS):
                        nc.tensor.matmul(ps_h1[t][m], w1_sb[0:n, c, cols], pairs_t[0:n, t % 2, c],
                                         start=(c == 0), stop=False)
                    nc.tensor.matmul(ps_h1[t][m], w1_sb[:, K1 - 1, cols], xt_sb[:, t * P:(t + 1) * P],
                                     start=False, stop=True).then_inc(h1_ready, 1)

            def layer2(t):
                if t >= 1:
                    pe.wait_ge(h2_stored, M2 * t)
                for m in range(M2):
                    if t >= 1 and m == (1 if t == TILES - 1 else 0):
                        pe.wait_ge(y_copied, t)
                    for c in range(M1):
                        if m == 0:
                            pe.wait_ge(h1_stored, M1 * t + c + 1)
                        last = nc.tensor.matmul(ps_h2[t][m], w2_sb[:, c, m * P:(m + 1) * P], h1[:, c],
                                                start=(c == 0), stop=(c == M1 - 1))
                    last.then_inc(h2_ready, 1)

            def layer3(t):
                for c in range(M2):
                    pe.wait_ge(h2_stored, M2 * t + (c + 1 if t == TILES - 1 else M2))
                    last = nc.tensor.matmul(ps_y[t], w3_sb[:, c:c + 1], h2[:, c],
                                            start=(c == 0), stop=(c == M2 - 1))
                last.then_inc(y_ready, 1)

            pe.wait_ge(consts_ready, NUM_CONSTS)
            for _ in range(WARM_UP):
                nc.tensor.matmul(ps_inter[:, 0, 0, 0:P], ident[:], ident[:], start=True, stop=True)
            for k in range(NUM_SELECTED):
                select(k)
                for n in EARLY[k]:
                    transpose_pack(n)
            pe.wait_ge(pads_zeroed, 1)
            pe.wait_ge(dense_stored, 1)
            pe.wait_ge(embed_stored, NUM_SELECTED)
            pairs_use = {}
            for t in range(TILES):
                pe.wait_ge(trans_stored, uses_at_tile[t])
                late = late_packs(t)
                for s in range(SETS):
                    interact(t, s)
                    if s == 0 and t >= 2:
                        layer3(t - 2)
                    if s == 1 and t >= 1:
                        pairs_use[t - 1] = transpose_pairs(t - 1)
                    if s == 2 and 1 <= t < TILES - 1:
                        layer1(t - 1, pairs_use[t - 1])
                    for n in late[s]:
                        transpose_pack(n)
                    if s == 3 and 1 <= t < TILES - 1:
                        layer2(t - 1)
            t = TILES - 1
            layer1(t - 1, pairs_use[t - 1])
            pairs_use[t] = transpose_pairs(t)
            layer2(t - 1)
            layer1(t, pairs_use[t])
            layer3(t - 1)
            layer2(t)
            layer3(t)

        @block.scalar
        def _(act):
            trans_uses = [0]

            def split_high(k):
                act.wait_ge(table_loaded[k % RAW], 32 * (k // RAW + 1))
                if k >= SPLIT:
                    act.wait_ge(embed_ready, k - SPLIT + 1)
                nc.scalar.activation(high[0:TABLE_PARTS, k % SPLIT],
                                     raw[0:TABLE_PARTS, k % RAW],
                                     ACT.Copy).then_inc(high_ready, 1)

            def make_last_hot(k):
                c = CHUNKS - 1
                if k == 0:
                    act.wait_ge(consts_ready, NUM_CONSTS)
                act.wait_ge(ids_row_loaded[k % IDS], 16 * (k // IDS + 1))
                if k >= 1:
                    act.wait_ge(last_hot_ready, k)
                nc.scalar.activation(distance[0:TABLE_PARTS], ids_row[0:TABLE_PARTS, k % IDS], ACT.Abs,
                                     bias=row_of[0:TABLE_PARTS, c:c + 1], scale=-1.0
                                     ).then_inc(distance_ready, 1)
                act.wait_ge(distance_ready, k + 1)
                nc.scalar.activation(hot[0:TABLE_PARTS, k % SPLIT, c], distance[0:TABLE_PARTS], ACT.Relu,
                                     bias=1.0, scale=-1.0).then_inc(last_hot_ready, 1)

            def store_embed(k):
                act.wait_ge(embed_ready, k + 1)
                nc.scalar.activation(slot_of_all(k), by_group(ps_embed[:, k % 2]), ACT.Copy).then_inc(embed_stored, 1)

            def store_pack(n):
                t, f0, f1 = pack_features(n)
                u = trans_uses[0]
                trans_uses[0] += 1
                act.wait_ge(trans_ready, u + 1)
                slot = NUM_SELECTED + f0
                out = vecs[:, t, :, :, slot:slot + f1 - f0].rearrange("d g r f -> d f r g")
                bank = ps_trans[:, u % 2, 0:(f1 - f0) * P].rearrange("p (f r g) -> p f r g", f=f1 - f0, g=GROUPS)
                nc.scalar.activation(out, bank, ACT.Copy).then_inc(trans_stored, 1)

            def store_pairs(t):
                u = trans_uses[0]
                trans_uses[0] += 1
                act.wait_ge(trans_ready, u + 1)
                if t >= 2:
                    act.wait_ge(h1_ready, M1 * (t - 1))
                bank = ps_trans[:, u % 2, :].rearrange("p (f b) -> p f b", b=P)
                full = len(PAIR_CHUNKS) - 1
                rest = PAIR_CHUNKS[-1][1]
                nc.scalar.activation(pairs_t[:, t % 2, 0:full], bank[:, 0:full], ACT.Copy)
                nc.scalar.activation(pairs_t[0:rest, t % 2, full], bank[0:rest, full],
                                     ACT.Copy).then_inc(trans_stored, 1)

            def store_inter(t, s):
                n = t * SETS + s
                act.wait_ge(inter_ready, n + 1)
                if s == 0 and t >= 2:
                    act.wait_ge(squared, t - 1)
                for r in (2, 3):
                    last = nc.scalar.activation(*inter_block(t, s, r), ACT.Copy)
                last.then_inc(inter_stored_act, 1)

            def store_y(t):
                act.wait_ge(y_ready, t + 1)
                nc.scalar.activation(y_sb[:, t * P:(t + 1) * P], ps_y[t], ACT.Copy).then_inc(y_copied, 1)

            def relu1(t):
                if t >= 1:
                    act.wait_ge(h2_ready, M2 * t)
                for m in range(M1):
                    act.wait_ge(h1_ready, M1 * t + (m + 1 if t == TILES - 1 else M1))
                    nc.scalar.activation(h1[:, m], ps_h1[t][m], ACT.Relu, bias=b1_sb[:, m:m + 1]
                                         ).then_inc(h1_stored, 1)

            def relu2(t):
                if t >= 1:
                    act.wait_ge(y_ready, t)
                for m in range(M2):
                    act.wait_ge(h2_ready, M2 * t + (m + 1 if t == TILES - 1 else M2))
                    nc.scalar.activation(h2[:, m], ps_h2[t][m], ACT.Relu, bias=b2_sb[:, m:m + 1]
                                         ).then_inc(h2_stored, 1)

            split_high(0)
            make_last_hot(0)
            for k in range(NUM_SELECTED):
                if k + 1 < NUM_SELECTED:
                    split_high(k + 1)
                    make_last_hot(k + 1)
                if k == 0:
                    act.wait_ge(x_loaded, 16)
                    nc.scalar.activation(slot_of_all(SLOTS - 1), by_group(xt_sb[:]), ACT.Copy).then_inc(dense_stored, 1)
                store_embed(k)
                for n in EARLY[k]:
                    store_pack(n)
            act.wait_ge(weights_loaded, 16 * WEIGHT_DMAS)
            act.wait_ge(rows_zeroed, 1)
            for t in range(TILES):
                late = late_packs(t)
                for s in range(SETS):
                    if s == 3 and 1 <= t < TILES - 1:
                        relu1(t - 1)
                    if s == 0 and t >= 2:
                        relu2(t - 2)
                    store_inter(t, s)
                    if s == 0 and t >= 2:
                        store_y(t - 2)
                    if s == 1 and t >= 1:
                        store_pairs(t - 1)
                    for n in late[s]:
                        store_pack(n)
            t = TILES - 1
            relu1(t - 1)
            store_pairs(t)
            relu2(t - 1)
            relu1(t)
            store_y(t - 1)
            relu2(t)
            store_y(t)

        @block.vector
        def _(dve):
            def split_low(k):
                dve.wait_ge(high_ready, k + 1)
                nc.vector.tensor_sub(low[0:TABLE_PARTS, k % SPLIT],
                                     raw[0:TABLE_PARTS, k % RAW],
                                     high[0:TABLE_PARTS, k % SPLIT].bitcast(F32)
                                     ).then_inc(low_ready, 1)

            def make_hot(k):
                dve.wait_ge(ids_row_loaded[k % IDS], 16 * (k // IDS + 1))
                if k >= SPLIT:
                    dve.wait_ge(embed_ready, k - SPLIT + 1)
                for c in range(DVE_HOTS):
                    nc.vector.tensor_scalar(hot[0:TABLE_PARTS, k % SPLIT, c], ids_row[0:TABLE_PARTS, k % IDS],
                                            row_of[0:TABLE_PARTS, c:c + 1], None,
                                            ALU.is_equal).then_inc(hot_ready, 1)

            def store_inter(t, s):
                n = t * SETS + s
                dve.wait_ge(inter_ready, n + 1)
                for r in (0, 1):
                    last = nc.vector.tensor_copy(*inter_block(t, s, r))
                last.then_inc(inter_stored_dve, 1)

            def pack_pairs(t):
                dve.wait_ge(inter_stored_dve, SETS * (t + 1))
                dve.wait_ge(inter_stored_act, SETS * (t + 1))
                nc.vector.transpose(square, inter[:, t % 2]).then_inc(squared, 1)
                dve.wait_ge(squared, t + 1)
                out = packed[:, t % 2]
                last = nc.vector.tensor_copy(out[:, 0:RECT].rearrange("p (j i) -> p j i", i=LOW),
                                             square[:, LOW - 1:COLS, 0:LOW])
                at = RECT
                flat = square_room[:, :]
                step = LOW * QUAD + LOW
                for m in range(1, SLOTS - LOW):
                    first = (m - 1) * QUAD
                    if m < LOW:
                        out2 = out[:, at:at + 2 * m].rearrange("p (two i) -> p two i", two=2)
                        src2 = flat[:, first:first + 2 * step].rearrange("p (two x) -> p two x", two=2)
                        last = nc.vector.tensor_copy(out2, src2[:, :, 0:m])
                        at += 2 * m
                    else:
                        last = nc.vector.tensor_copy(out[:, at:at + m], flat[:, first + step:first + step + m])
                        at += m
                last.then_inc(pairs_packed, 1)

            dve.wait_ge(consts_ready, NUM_CONSTS)
            nc.vector.memset(vecs[:].rearrange("d t g r s -> d (t g r) s")[:, :, SLOTS:QUAD], 0.0).then_inc(pads_zeroed, 1)
            for k in range(NUM_SELECTED):
                make_hot(k)
                split_low(k)
            nc.vector.memset(inter[P - QUAD:P], 0.0).then_inc(rows_zeroed, 1)
            for t in range(TILES):
                for s in range(SETS):
                    store_inter(t, s)
                pack_pairs(t)


def kernel(**inputs):
    import numpy as np
    import concourse.bacc as bacc
    from concourse.bass_utils import run_bass_kernel_spmd as run

    a = {k: np.asarray(v) for k, v in inputs.items()}
    arrays = {
        "x_t": np.ascontiguousarray(a["r_dense_x"].T),
        "ids": np.ascontiguousarray(a["ids"]),
        "ids_t": np.ascontiguousarray(a["ids"].T),
        "w1": np.ascontiguousarray(a["W_top1"][first_layer_rows()]),
        "w2": np.ascontiguousarray(a["W_top2"]),
        "small": np.ascontiguousarray(np.concatenate(
            [a["b_top1"].reshape(M1, P).T, a["b_top2"].reshape(M2, P).T, a["W_top3"].reshape(M2, P).T], axis=1)),
    }
    for f in range(FEATS):
        arrays[f"table{f}"] = np.ascontiguousarray(a[f"tbl_{f}"])

    nc = bacc.Bacc("TRN2", target_bir_lowering=False, num_devices=1)
    dram = {name: nc.dram_tensor(name, v.shape, mybir.dt.from_np(v.dtype), kind="ExternalInput").ap()
            for name, v in arrays.items()}
    y = nc.dram_tensor("y", (1, BATCH), F32, kind="ExternalOutput").ap()
    dlrm_kernel(nc, dram["x_t"], dram["ids"], dram["ids_t"], [dram[f"table{f}"] for f in range(FEATS)],
                dram["w1"], dram["w2"], dram["small"], y)
    return run(nc, [arrays], core_ids=[0]).results[0]["y"].reshape(BATCH, 1)
```
